# Optimizing a Trainium2 kernel written in Bass

```python
import numpy as np
import jax
import jax.numpy as jnp

def _softmax(x, axis=-1):
    return jax.nn.softmax(x, axis=axis)

def _gelu(x):
    return jax.nn.gelu(x, approximate=True)

def _silu(x):
    return jax.nn.silu(x)

def _sigmoid(x):
    return jax.nn.sigmoid(x)

def _layernorm(x, axis=-1, eps=1e-05):
    m = jnp.mean(x, axis=axis, keepdims=True)
    v = jnp.var(x, axis=axis, keepdims=True)
    return (x - m) / jnp.sqrt(v + eps)

def _scatter_add(tgt, idx, src, axis=0):
    return tgt.at[idx].add(src)

def _segment_sum(src, seg, n):
    return jax.ops.segment_sum(src, seg, n)
kernel_name = 'mk_dlrm_tower_d1_rec_r8_10e807'

def setup_inputs(seed: int=0):
    np.random.seed(seed)
    _w = jnp.asarray

    def _rec_inputs():
        import jax
        import jax.numpy as jnp
        _tk = jax.random.key(seed)
        ids = jnp.stack([jax.random.randint(jax.random.fold_in(_tk, 200 + f), (2048,), 0, v, jnp.int32) for f, v in enumerate([1000, 1250, 1250, 125000, 12500, 12500, 1250, 1000, 12500, 1250, 1250, 1250, 1250, 1250, 12500, 1000, 1000, 1250, 1250, 1250, 12500, 1000, 1250, 1250, 12500, 1000])], axis=1)
        tbl_0 = 0.05 * jax.random.normal(jax.random.fold_in(_tk, 500 + 0), (1000, 128), jnp.float32)
        tbl_1 = 0.05 * jax.random.normal(jax.random.fold_in(_tk, 500 + 1), (1250, 128), jnp.float32)
        tbl_2 = 0.05 * jax.random.normal(jax.random.fold_in(_tk, 500 + 2), (1250, 128), jnp.float32)
        tbl_3 = 0.05 * jax.random.normal(jax.random.fold_in(_tk, 500 + 3), (125000, 128), jnp.float32)
        tbl_4 = 0.05 * jax.random.normal(jax.random.fold_in(_tk, 500 + 4), (12500, 128), jnp.float32)
        tbl_5 = 0.05 * jax.random.normal(jax.random.fold_in(_tk, 500 + 5), (12500, 128), jnp.float32)
        tbl_6 = 0.05 * jax.random.normal(jax.random.fold_in(_tk, 500 + 6), (1250, 128), jnp.float32)
        tbl_7 = 0.05 * jax.random.normal(jax.random.fold_in(_tk, 500 + 7), (1000, 128), jnp.float32)
        tbl_8 = 0.05 * jax.random.normal(jax.random.fold_in(_tk, 500 + 8), (12500, 128), jnp.float32)
        tbl_9 = 0.05 * jax.random.normal(jax.random.fold_in(_tk, 500 + 9), (1250, 128), jnp.float32)
        tbl_10 = 0.05 * jax.random.normal(jax.random.fold_in(_tk, 500 + 10), (1250, 128), jnp.float32)
        tbl_11 = 0.05 * jax.random.normal(jax.random.fold_in(_tk, 500 + 11), (1250, 128), jnp.float32)
        tbl_12 = 0.05 * jax.random.normal(jax.random.fold_in(_tk, 500 + 12), (1250, 128), jnp.float32)
        tbl_13 = 0.05 * jax.random.normal(jax.random.fold_in(_tk, 500 + 13), (1250, 128), jnp.float32)
        tbl_14 = 0.05 * jax.random.normal(jax.random.fold_in(_tk, 500 + 14), (12500, 128), jnp.float32)
        tbl_15 = 0.05 * jax.random.normal(jax.random.fold_in(_tk, 500 + 15), (1000, 128), jnp.float32)
        tbl_16 = 0.05 * jax.random.normal(jax.random.fold_in(_tk, 500 + 16), (1000, 128), jnp.float32)
        tbl_17 = 0.05 * jax.random.normal(jax.random.fold_in(_tk, 500 + 17), (1250, 128), jnp.float32)
        tbl_18 = 0.05 * jax.random.normal(jax.random.fold_in(_tk, 500 + 18), (1250, 128), jnp.float32)
        tbl_19 = 0.05 * jax.random.normal(jax.random.fold_in(_tk, 500 + 19), (1250, 128), jnp.float32)
        tbl_20 = 0.05 * jax.random.normal(jax.random.fold_in(_tk, 500 + 20), (12500, 128), jnp.float32)
        tbl_21 = 0.05 * jax.random.normal(jax.random.fold_in(_tk, 500 + 21), (1000, 128), jnp.float32)
        tbl_22 = 0.05 * jax.random.normal(jax.random.fold_in(_tk, 500 + 22), (1250, 128), jnp.float32)
        tbl_23 = 0.05 * jax.random.normal(jax.random.fold_in(_tk, 500 + 23), (1250, 128), jnp.float32)
        tbl_24 = 0.05 * jax.random.normal(jax.random.fold_in(_tk, 500 + 24), (12500, 128), jnp.float32)
        tbl_25 = 0.05 * jax.random.normal(jax.random.fold_in(_tk, 500 + 25), (1000, 128), jnp.float32)
        _rk = jax.random.fold_in(_tk, 7)
        r_dense_features = -0.000520686 + 1.00062 * jax.random.normal(jax.random.fold_in(_rk, 101), (2048, 128), jnp.float32)
        W_top1 = 0.0405887 * jax.random.normal(jax.random.fold_in(_tk, 801), (607, 512), jnp.float32)
        W_top2 = 0.0441942 * jax.random.normal(jax.random.fold_in(_tk, 802), (512, 256), jnp.float32)
        W_top3 = 0.0625 * jax.random.normal(jax.random.fold_in(_tk, 803), (256, 1), jnp.float32)
        b_top1 = jnp.zeros((512,), jnp.float32)
        b_top2 = jnp.zeros((256,), jnp.float32)
        return (r_dense_features, ids, tbl_0, tbl_1, tbl_2, tbl_3, tbl_4, tbl_5, tbl_6, tbl_7, tbl_8, tbl_9, tbl_10, tbl_11, tbl_12, tbl_13, tbl_14, tbl_15, tbl_16, tbl_17, tbl_18, tbl_19, tbl_20, tbl_21, tbl_22, tbl_23, tbl_24, tbl_25, W_top1, b_top1, W_top2, b_top2, W_top3)
    r_dense_features, ids, tbl_0, tbl_1, tbl_2, tbl_3, tbl_4, tbl_5, tbl_6, tbl_7, tbl_8, tbl_9, tbl_10, tbl_11, tbl_12, tbl_13, tbl_14, tbl_15, tbl_16, tbl_17, tbl_18, tbl_19, tbl_20, tbl_21, tbl_22, tbl_23, tbl_24, tbl_25, W_top1, b_top1, W_top2, b_top2, W_top3 = _rec_inputs()

    def _L0_rec_setup():
        import jax, jax.numpy as jnp
        import numpy as np
        B, F, D = (2048, 26, 128)
        key = jax.random.key(seed)
        k1, k2 = jax.random.split(key)
        dense_features = jax.random.normal(k1, (B, D), dtype=jnp.float32)
        sparse_values = jax.random.normal(k2, (B, F, D), dtype=jnp.float32)
        return {'dense_features': dense_features, 'sparse_values': sparse_values}
    _L0_rec_all = _L0_rec_setup()
    _L0_rec_in = {k: v for k, v in _L0_rec_all.items() if k in ()}
    del _L0_rec_all
    return {'r_dense_features': r_dense_features, 'ids': ids, 'tbl_0': tbl_0, 'tbl_1': tbl_1, 'tbl_2': tbl_2, 'tbl_3': tbl_3, 'tbl_4': tbl_4, 'tbl_5': tbl_5, 'tbl_6': tbl_6, 'tbl_7': tbl_7, 'tbl_8': tbl_8, 'tbl_9': tbl_9, 'tbl_10': tbl_10, 'tbl_11': tbl_11, 'tbl_12': tbl_12, 'tbl_13': tbl_13, 'tbl_14': tbl_14, 'tbl_15': tbl_15, 'tbl_16': tbl_16, 'tbl_17': tbl_17, 'tbl_18': tbl_18, 'tbl_19': tbl_19, 'tbl_20': tbl_20, 'tbl_21': tbl_21, 'tbl_22': tbl_22, 'tbl_23': tbl_23, 'tbl_24': tbl_24, 'tbl_25': tbl_25, 'W_top1': W_top1, 'b_top1': b_top1, 'W_top2': W_top2, 'b_top2': b_top2, 'W_top3': W_top3}

def reference(r_dense_features, ids, tbl_0, tbl_1, tbl_2, tbl_3, tbl_4, tbl_5, tbl_6, tbl_7, tbl_8, tbl_9, tbl_10, tbl_11, tbl_12, tbl_13, tbl_14, tbl_15, tbl_16, tbl_17, tbl_18, tbl_19, tbl_20, tbl_21, tbl_22, tbl_23, tbl_24, tbl_25, W_top1, b_top1, W_top2, b_top2, W_top3):
    import jax
    import jax.numpy as jnp

    def _L0_rec_ref(dense_features, sparse_values):
        import jax, jax.numpy as jnp
        import numpy as np
        B, F, D = (2048, 26, 128)
        sd = jnp.einsum('bfd,bd->bf', sparse_values, dense_features)
        ss = jnp.einsum('bfd,bgd->bfg', sparse_values, sparse_values)
        iu, ju = jnp.triu_indices(F, k=1)
        pairs = ss[:, iu, ju]
        return jnp.concatenate([dense_features, sd, pairs], axis=1)
    e = jnp.stack([tbl_0[ids[:, 0]], tbl_1[ids[:, 1]], tbl_2[ids[:, 2]], tbl_3[ids[:, 3]], tbl_4[ids[:, 4]], tbl_5[ids[:, 5]], tbl_6[ids[:, 6]], tbl_7[ids[:, 7]], tbl_8[ids[:, 8]], tbl_9[ids[:, 9]], tbl_10[ids[:, 10]], tbl_11[ids[:, 11]], tbl_12[ids[:, 12]], tbl_13[ids[:, 13]], tbl_14[ids[:, 14]], tbl_15[ids[:, 15]], tbl_16[ids[:, 16]], tbl_17[ids[:, 17]], tbl_18[ids[:, 18]], tbl_19[ids[:, 19]], tbl_20[ids[:, 20]], tbl_21[ids[:, 21]], tbl_22[ids[:, 22]], tbl_23[ids[:, 23]], tbl_24[ids[:, 24]], tbl_25[ids[:, 25]]], axis=1)
    z = _L0_rec_ref(r_dense_features, e)
    z = z.reshape(z.shape[0], -1)
    h = jnp.concatenate([z, r_dense_features], axis=1)
    h = jnp.maximum(h @ W_top1 + b_top1, 0.0)
    h = jnp.maximum(h @ W_top2 + b_top2, 0.0)
    y = h @ W_top3
    return y

_drawn_inputs = setup_inputs


def setup_inputs(seed=0):
    import zlib

    import numpy as np

    out = dict(_drawn_inputs(seed))
    spreads = {'b_top1': (0.0, 0.1), 'b_top2': (0.0, 0.1)}
    factors = {}
    for name, (base, spread) in spreads.items():
        noise = np.random.default_rng([zlib.crc32(name.encode()), seed]).standard_normal(out[name].shape)
        drawn = base * np.exp(spread * noise) if base else spread * noise
        out[name] = jnp.asarray(drawn.astype(out[name].dtype))
    for name, factor in factors.items():
        out[name] = (out[name] * factor).astype(out[name].dtype)
    return out
```

```python
import concourse.bass as bass
from concourse import mybir
from contextlib import ExitStack

F32 = mybir.dt.float32
I32 = mybir.dt.int32
ACT = mybir.ActivationFunctionType
ALU = mybir.AluOpType

P = 128
TABLES = 26
VECS = TABLES + 1
SLOTS = 32
SHIFTS = (VECS - 1) // 2
PAIRS = VECS * SHIFTS
VECS_PER_CHUNK = 9
CHUNKS = VECS // VECS_PER_CHUNK
CHUNK = VECS_PER_CHUNK * SHIFTS
GROUP = 4
GROUPS = [list(range(g, min(g + GROUP, VECS))) for g in range(0, VECS, GROUP)]
QUADS = P // 4
FILLS = 4
PER_BANK = QUADS // FILLS // 2


def pair_rows():
    rows = []
    for v in range(VECS):
        for k in range(1, SHIFTS + 1):
            a, b = sorted((v, (v + k) % VECS))
            if b == TABLES:
                rows.append(P + a)
            else:
                rows.append(P + TABLES + a * TABLES - a * (a + 1) // 2 + b - a - 1)
    return rows


def dlrm_tower(nc, dense, ids, tables, w1_pairs, w1_dense, b1, w2, b2, w3, eye, out):
    B = dense.shape[0]
    TILES = B // P
    ROUNDS = TILES // 2
    H1, H2 = w2.shape
    M1, M2 = H1 // P, H2 // P

    dense_v = dense.rearrange("(p t) d -> p t d", t=TILES)
    ids_v = ids.rearrange("(p t) f -> p t f", t=TILES)
    out_v = out.rearrange("(p t) o -> p (t o)", t=TILES)

    ctx = ExitStack()
    with ctx:
        def sb(name, shape, dt=F32):
            return ctx.enter_context(nc.sbuf_tensor(name, shape, dt))

        def pb(name, shape):
            return ctx.enter_context(nc.psum_tensor(name, shape, F32))

        def sem(name):
            return ctx.enter_context(nc.semaphore(name))

        ident = sb("ident", [P, P])
        w1p = sb("w1p", [CHUNK, CHUNKS, H1])
        w1d2 = sb("w1d2", [P, 2, H1])
        w1d = sb("w1d", [P, H1])
        w2s = sb("w2s", [P, M1, H2])
        w3s = sb("w3s", [P, M2])
        b1s = sb("b1s", [P, M1])
        b2s = sb("b2s", [P, M2])
        idx = [sb(f"idx{s}", [P, TABLES], I32) for s in range(2)]
        rows = [sb(f"rows{s}", [P, VECS, P]) for s in range(2)]
        vecs = [sb(f"vecs{s}", [P, P, SLOTS]) for s in range(2)]
        blocks = sb("blocks", [P, QUADS, VECS])
        dots = sb("dots", [P, VECS + SHIFTS, SLOTS])
        packed = sb("packed", [P, PAIRS])
        pairs = sb("pairs", [CHUNK, CHUNKS, P])
        h1 = sb("h1", [P, M1, P])
        h2 = sb("h2", [P, M2, P])
        y = sb("y", [P, TILES])

        shifted = dots[:, :, :].rearrange("p a b -> p (a b)")
        shifted = bass.AP(tensor=shifted.tensor, offset=shifted.offset + SLOTS,
                          ap=[list(shifted.ap[0]), [SLOTS + 1, VECS], [SLOTS, SHIFTS]])

        turned = [pb(f"turned{b}", [P, GROUP, P]) for b in range(2)]
        gram = [pb(f"gram{b}", [P, 2, 512]) for b in range(2)]
        small = pb("small", [P, 512])
        pre1 = pb("pre1", [P, M1, P])
        pairs_ps = small[0:CHUNK, 0:CHUNKS * P].rearrange("p (c s) -> p c s", c=CHUNKS)
        pre2 = small[:, 0:M2 * P].rearrange("p (m s) -> p m s", m=M2)
        y_ps = small[:, 511:512]

        weights_landed = sem("weights_landed")
        idx_landed = [sem(f"idx_landed{s}") for s in range(2)]
        dense_landed = [sem(f"dense_landed{s}") for s in range(2)]
        rows_landed = [[sem(f"rows_landed{s}_{g}") for g in range(len(GROUPS))] for s in range(2)]
        gathers_begun = sem("gathers_begun")
        w1d_summed = sem("w1d_summed")
        vecs_zeroed = sem("vecs_zeroed")
        turned_full = [sem(f"turned_full{b}") for b in range(2)]
        turned_kept = [sem(f"turned_kept{b}") for b in range(2)]
        gram_full = [sem(f"gram_full{b}") for b in range(2)]
        gram_kept = [sem(f"gram_kept{b}") for b in range(2)]
        rows_used = [sem(f"rows_used{s}") for s in range(2)]
        dots_ready = sem("dots_ready")
        packed_ready = sem("packed_ready")
        pairs_full = sem("pairs_full")
        pairs_kept = sem("pairs_kept")
        pre1_full = sem("pre1_full")
        h1_ready = sem("h1_ready")
        pre2_full = sem("pre2_full")
        h2_ready = sem("h2_ready")
        y_full = sem("y_full")
        y_kept = sem("y_kept")
        stored = sem("stored")

        WEIGHT_DMAS = 7
        ROUND_GROUPS = 2 * len(GROUPS)
        BANK_USES = ROUND_GROUPS // 2

        block = ctx.enter_context(nc.Block())

        @block.sync
        def _(sp):
            with sp.Fori(0, ROUNDS) as i:
                for s in range(2):
                    sp.wait_ge(rows_used[s], i + 1)
                    sp.dma_start(idx[s][:, :], ids_v[:, i * 2 + s, :]).then_inc(idx_landed[s], 16)
                    sp.dma_start(rows[s][:, TABLES, :], dense_v[:, i * 2 + s, :]).then_inc(dense_landed[s], 16)
            sp.wait_ge(y_kept, 1 + TILES)
            sp.dma_start(out_v, y[:, :]).then_inc(stored, 16)
            sp.wait_ge(stored, 16)

        @block.gpsimd
        def _(pool):
            for free in (*rows_used, *turned_kept, *gram_kept, dots_ready, y_kept):
                pool.sem_inc(free, 1)
            with pool.Fori(0, ROUNDS) as i:
                for s in range(2):
                    pool.wait_ge(idx_landed[s], (i + 1) * 16)
                    pool.sem_inc(gathers_begun, 1)
                    for g, group in enumerate(GROUPS):
                        for v in group:
                            if v < TABLES:
                                pool.indirect_dma_start(
                                    rows[s][:, v, :], None, tables[v],
                                    bass.IndirectOffsetOnAxis(ap=idx[s][:, v:v + 1], axis=0),
                                ).then_inc(rows_landed[s][g], 16)

        def keep_turned(eng, copy, i, s, bank):
            for g, group in enumerate(GROUPS):
                r = s * len(GROUPS) + g
                if r % 2 == bank:
                    eng.wait_ge(turned_full[bank], i * BANK_USES + (r // 2 + 1))
                    dst = vecs[s][:, :, group[0]:group[-1] + 1].rearrange("p (q j) v -> p v j q", j=4)
                    src = turned[bank][:, 0:len(group), :].rearrange("p v (j q) -> p v j q", j=4)
                    copy(dst, src).then_inc(turned_kept[bank], 1)

        def keep_gram(eng, copy, i, s, quadrants):
            for n in range(FILLS):
                eng.wait_ge(gram_full[n % 2], i * FILLS + (s * FILLS // 2 + n // 2 + 1))
                if n == 0:
                    eng.wait_ge(dots_ready, i * 2 + (1 + s))
                for j in quadrants:
                    src = gram[n % 2][32 * j:32 * j + 32, :, 0:PER_BANK * 4 * VECS]
                    src = src.rearrange("p b (q j v) -> p b q j v", j=4, v=VECS)[:, :, :, j, :]
                    q0 = n * 2 * PER_BANK
                    dst = blocks[32 * j:32 * j + 32, q0:q0 + 2 * PER_BANK, :]
                    last = copy(dst.rearrange("p (b q) v -> p b q v", b=2), src)
                last.then_inc(gram_kept[n % 2], 1)

        @block.scalar
        def _(act):
            act.dma_start(ident[:, :], eye).then_inc(weights_landed, 16)
            act.dma_start(w1d2[:, :, :], w1_dense.rearrange("(a p) n -> p a n", a=2)).then_inc(weights_landed, 16)
            act.dma_start(w1p[:, :, :], w1_pairs.rearrange("(c p) n -> p c n", c=CHUNKS)).then_inc(weights_landed, 16)
            act.dma_start(w2s[:, :, :], w2.rearrange("(c p) n -> p c n", p=P)).then_inc(weights_landed, 16)
            with nc.allow_non_contiguous_dma(reason="a few hundred words, once"):
                act.dma_start(b1s[:, :], b1.rearrange("(c p) -> p c", p=P)).then_inc(weights_landed, 16)
                act.dma_start(b2s[:, :], b2.rearrange("(c p) -> p c", p=P)).then_inc(weights_landed, 16)
                act.dma_start(w3s[:, :], w3.rearrange("(c p) o -> p (c o)", p=P)).then_inc(weights_landed, 16)
            act.wait_ge(vecs_zeroed, 2)
            act.wait_ge(weights_landed, 16 * WEIGHT_DMAS)
            with act.Fori(0, ROUNDS) as i:
                for s in range(2):
                    keep_turned(act, nc.scalar.copy, i, s, 1)
                    keep_gram(act, nc.scalar.copy, i, s, (0, 1))
                    act.wait_ge(dots_ready, i * 2 + (1 + s + 1))
                    nc.scalar.copy(packed[:, :].rearrange("p (v k) -> p v k", k=SHIFTS),
                                   shifted).then_inc(packed_ready, 1)
                    act.wait_ge(pairs_full, i * 2 + (s + 1))
                    nc.scalar.copy(pairs[:, :, :], pairs_ps).then_inc(pairs_kept, 1)
                    act.wait_ge(pre1_full, i * 2 + (s + 1))
                    for m in range(M1):
                        nc.scalar.activation(h1[:, m, :], pre1[:, m, :], ACT.Relu,
                                             bias=b1s[:, m:m + 1]).then_inc(h1_ready, 1)

        @block.vector
        def _(dve):
            for s in range(2):
                nc.vector.memset(vecs[s][:, :, :], 0.0).then_inc(vecs_zeroed, 1)
            dve.wait_ge(vecs_zeroed, 2)
            dve.wait_ge(weights_landed, 16 * WEIGHT_DMAS)
            nc.vector.tensor_tensor(w1d[:, :], w1d2[:, 0, :], w1d2[:, 1, :], ALU.add).then_inc(w1d_summed, 1)
            with dve.Fori(0, ROUNDS) as i:
                for s in range(2):
                    keep_turned(dve, nc.vector.tensor_copy, i, s, 0)
                    keep_gram(dve, nc.vector.tensor_copy, i, s, (2, 3))
                    for b in range(2):
                        dve.wait_ge(gram_kept[b], i * (2 * FILLS) + (1 + (s + 1) * FILLS))
                    by_vec = blocks[:, :, :].rearrange("p q v -> p v q")
                    nc.vector.transpose(dots[:, 0:VECS, :], by_vec)
                    nc.vector.transpose(dots[:, VECS:VECS + SHIFTS, :], by_vec[:, 0:SHIFTS, :]).then_inc(dots_ready, 1)
                    dve.wait_ge(pre2_full, i * 2 + (s + 1))
                    for m in range(M2):
                        nc.vector.tensor_scalar(h2[:, m, :], pre2[:, m, :], b2s[:, m:m + 1], 0.0,
                                                ALU.add, ALU.max).then_inc(h2_ready, 1)
                    dve.wait_ge(y_full, i * 2 + (s + 1))
                    nc.vector.tensor_copy(y[:, bass.ds(i * 2 + s, 1)], y_ps).then_inc(y_kept, 1)

        @block.tensor
        def _(pe):
            pe.wait_ge(weights_landed, 16 * WEIGHT_DMAS)
            pe.wait_ge(w1d_summed, 1)
            pe.wait_ge(vecs_zeroed, 2)
            with pe.Fori(0, ROUNDS) as i:
                for s in range(2):
                    for g, group in enumerate(GROUPS):
                        r = s * len(GROUPS) + g
                        n = sum(v < TABLES for v in group)
                        pe.wait_ge(rows_landed[s][g], i * (16 * n) + 16 * n)
                        if TABLES in group:
                            pe.wait_ge(dense_landed[s], i * 16 + 16)
                        pe.wait_ge(turned_kept[r % 2], i * BANK_USES + (1 + r // 2))
                        for k, v in enumerate(group):
                            last = nc.tensor.transpose(turned[r % 2][:, k, :], rows[s][:, v, :], ident[:, :])
                        last.then_inc(turned_full[r % 2], 1)
                    for b in range(2):
                        used = len([r for r in range((s + 1) * len(GROUPS)) if r % 2 == b])
                        pe.wait_ge(turned_kept[b], i * BANK_USES + (1 + used))
                    four = vecs[s][:, :, :].rearrange("p (q j) v -> p q j v", j=4)
                    for n in range(FILLS):
                        pe.wait_ge(gram_kept[n % 2], i * (2 * FILLS) + (1 + s * FILLS + n // 2 * 2))
                        for b in range(2):
                            for k in range(PER_BANK):
                                q = (n * 2 + b) * PER_BANK + k
                                last = nc.tensor.matmul(
                                    gram[n % 2][:, b, k * 4 * VECS:(k + 1) * 4 * VECS],
                                    four[:, q, :, :].rearrange("p j v -> p (j v)"), four[:, q, :, 0:VECS], start=True, stop=True)
                        last.then_inc(gram_full[n % 2], 1)
                    pe.wait_ge(packed_ready, i * 2 + (s + 1))
                    pe.wait_ge(y_kept, i * 2 + (1 + s))
                    for c in range(CHUNKS):
                        last = nc.tensor.transpose(pairs_ps[:, c, :], packed[:, c * CHUNK:(c + 1) * CHUNK], ident[:, :])
                        if c == 0:
                            last.then_inc(rows_used[s], 1)
                    last.then_inc(pairs_full, 1)
                    pe.wait_ge(pairs_kept, i * 2 + (s + 1))
                    dense_t = vecs[s][:, :, TABLES].rearrange("p (q j) -> p j q", j=4)
                    for m in range(M1):
                        nc.tensor.matmul(pre1[:, m, :], w1d[:, m * P:(m + 1) * P], dense_t,
                                         start=True, stop=False)
                        for c in range(CHUNKS):
                            last = nc.tensor.matmul(pre1[:, m, :], w1p[:, c, m * P:(m + 1) * P], pairs[:, c, :],
                                                    start=False, stop=(c == CHUNKS - 1))
                    last.then_inc(pre1_full, 1)
                    for m in range(M2):
                        for c in range(M1):
                            if m == 0:
                                pe.wait_ge(h1_ready, i * (2 * M1) + (s * M1 + c + 1))
                            last = nc.tensor.matmul(pre2[:, m, :], w2s[:, c, m * P:(m + 1) * P], h1[:, c, :],
                                                    start=(c == 0), stop=(c == M1 - 1))
                    last.then_inc(pre2_full, 1)
                    for c in range(M2):
                        if c == 0:
                            pe.wait_ge(h2_ready, i * (2 * M2) + (s + 1) * M2)
                        last = nc.tensor.matmul(y_ps, h2[:, c, :], w3s[:, c:c + 1], start=(c == 0), stop=(c == M2 - 1))
                    last.then_inc(y_full, 1)




def kernel(**inputs):
    import numpy as _np
    import concourse.bacc as _bacc
    from concourse import mybir as _mybir
    from concourse.bass_utils import run_bass_kernel_spmd as _run

    x = {name: _np.asarray(a) for name, a in inputs.items()}
    w1 = x["W_top1"]
    given = {"dense": x["r_dense_features"], "ids": x["ids"]}
    given |= {f"table{f}": x[f"tbl_{f}"] for f in range(TABLES)}
    given |= {"w1_pairs": w1[_np.array(pair_rows())],
              "w1_dense": _np.concatenate([w1[:P], w1[-P:]]),
              "b1": x["b_top1"], "w2": x["W_top2"], "b2": x["b_top2"], "w3": x["W_top3"],
              "eye": _np.eye(P, dtype=_np.float32)}
    nc = _bacc.Bacc("TRN2", target_bir_lowering=False, num_devices=1)
    aps, arrays = {}, {}
    for name, a in given.items():
        a = _np.ascontiguousarray(a)
        arrays[f"in_{name}"] = a
        aps[name] = nc.dram_tensor(f"in_{name}", a.shape, _mybir.dt.from_np(a.dtype), kind="ExternalInput").ap()
    out = nc.dram_tensor("out_y", (x["ids"].shape[0], 1), _mybir.dt.float32, kind="ExternalOutput").ap()
    dlrm_tower(nc, aps["dense"], aps["ids"], [aps[f"table{f}"] for f in range(TABLES)], aps["w1_pairs"],
               aps["w1_dense"], aps["b1"], aps["w2"], aps["b2"], aps["w3"], aps["eye"], out)
    r = _run(nc, [arrays], core_ids=[0])
    return r.results[0]["out_y"]
```

```python
import concourse.bass as bass
from concourse import mybir
from contextlib import ExitStack

F32 = mybir.dt.float32
BF16 = mybir.dt.bfloat16
F16 = mybir.dt.float16
I32 = mybir.dt.int32
ACT = mybir.ActivationFunctionType
ALU = mybir.AluOpType

P = 128
TABLES = 26
VECS = TABLES + 1
SLOTS = 32
SHIFTS = (VECS - 1) // 2
PAIRS = VECS * SHIFTS
VECS_PER_CHUNK = 9
CHUNKS = VECS // VECS_PER_CHUNK
CHUNK = VECS_PER_CHUNK * SHIFTS
QUADS = P // 4
PER_FILL = 4
FILLS = QUADS // PER_FILL

PICKED = [0, 7, 15, 16]
ROWS = 1000
PARTS = 8
ROWS_PER_PART = ROWS // PARTS
SPLIT = 3
GATHERED = [f for f in range(TABLES) if f not in PICKED]
DENSE = len(GATHERED)
ORDER = [*GATHERED, TABLES, *PICKED]
GROUP = 4
GROUPS = [list(range(g, min(g + GROUP, DENSE + 1))) for g in range(0, DENSE + 1, GROUP)]
NG = len(GROUPS)
NP = len(PICKED)
EARLY = 2

L1_GAP, TURN_GAP, PLACE_GAP, GRAM_GAP = range(4)
GAPS = 4
TURN_GAP_AFTER = 1
L2_AFTER = 3
PICKS = NP * PARTS * SPLIT
PICK_SHARES = [7, 6, 12]
PICK_SHARES.append(PICKS // 2 - sum(PICK_SHARES))
PICK_AT = [sum((PICK_SHARES * 2)[:k]) for k in range(2 * GAPS + 1)]


def picks_complete(s, *gaps):
    per_table = PARTS * SPLIT
    return [k for g in gaps for k in range(NP)
            if PICK_AT[s * GAPS + g] < (k + 1) * per_table <= PICK_AT[s * GAPS + g + 1]]


SPLIT_ORDER = [(k, a) for k0 in range(0, NP, 2) for a in range(SPLIT) for k in range(k0, min(k0 + 2, NP))]
TAKEN_ORDER = [(k, a) for k, a in SPLIT_ORDER if a < SPLIT - 1]


def pair_rows():
    rows = []
    for v in range(VECS):
        for k in range(1, SHIFTS + 1):
            a, b = sorted((ORDER[v], ORDER[(v + k) % VECS]))
            if b == TABLES:
                rows.append(P + a)
            else:
                rows.append(P + TABLES + a * TABLES - a * (a + 1) // 2 + b - a - 1)
    return rows


def dlrm_tower(nc, dense, ids, picked_ids, tables, w1_pairs, w1_dense, b1, w2, b2, w3, eye, row_of, out):
    B = dense.shape[0]
    TILES = B // P
    ROUNDS = TILES // 2
    WIDE = 2 * P
    H1, H2 = w2.shape
    M1, M2 = H1 // P, H2 // P

    dense_v = dense.rearrange("(p t) d -> p t d", t=TILES)
    ids_v = ids.rearrange("(p t) f -> p t f", t=TILES)
    out_v = out.rearrange("b o -> o b")

    ctx = ExitStack()
    with ctx:
        def sb(name, shape, dt=F32):
            return ctx.enter_context(nc.sbuf_tensor(name, shape, dt))

        def pb(name, shape):
            return ctx.enter_context(nc.psum_tensor(name, shape, F32))

        def sem(name):
            return ctx.enter_context(nc.semaphore(name))

        ident = sb("ident", [P, P])
        rowid = sb("rowid", [ROWS_PER_PART, PARTS])
        w1p = sb("w1p", [CHUNK, CHUNKS, H1])
        w1d2 = sb("w1d2", [P, 2, H1])
        w1d = sb("w1d", [P, H1])
        w2s = sb("w2s", [P, M1, H2])
        w3s = sb("w3s", [P, M2])
        b1s = sb("b1s", [P, M1])
        b2s = sb("b2s", [P, M2])
        idx = [sb(f"idx{s}", [P, TABLES], I32) for s in range(2)]
        rows = [sb(f"rows{s}", [P, DENSE + 1, P]) for s in range(2)]
        vecs = [sb(f"vecs{s}", [P, P, SLOTS]) for s in range(2)]
        blocks = sb("blocks", [P, QUADS, VECS])
        dots = sb("dots", [P, VECS + SHIFTS, SLOTS])
        packed = sb("packed", [P, PAIRS])
        pairs = sb("pairs", [CHUNK, CHUNKS, P])
        h1 = sb("h1", [P, M1, P])
        h2 = sb("h2", [P, M2, P])
        y = sb("y", [1, P, TILES])
        idb = sb("idb", [ROWS_PER_PART, NP, WIDE], I32)
        idh = sb("idh", [ROWS_PER_PART, NP, WIDE], F16)
        onehot = [sb(f"onehot{k}", [ROWS_PER_PART, PARTS, WIDE], BF16) for k in range(NP)]
        parts = [sb(f"parts{k}", [ROWS_PER_PART, PARTS, SPLIT, P], BF16) for k in range(NP)]
        picks = sb("picks", [P, NP, WIDE])
        left = [sb(f"left{k}", [ROWS_PER_PART, PARTS, P]) for k in range(NP)]

        shifted = dots[:, :, :].rearrange("p a b -> p (a b)")
        shifted = bass.AP(tensor=shifted.tensor, offset=shifted.offset + SLOTS,
                          ap=[list(shifted.ap[0]), [SLOTS + 1, VECS], [SLOTS, SHIFTS]])

        turned = [pb(f"turned{b}", [P, GROUP, P]) for b in range(2)]
        gram = [pb(f"gram{b}", [P, 512]) for b in range(2)]
        picked = [pb(f"picked{b}", [P, 512]) for b in range(2)]
        small = pb("small", [P, 512])
        pre1 = pb("pre1", [P, M1, P])
        pairs_ps = small[0:CHUNK, 0:CHUNKS * P].rearrange("p (c s) -> p c s", c=CHUNKS)
        pre2 = small[:, 0:M2 * P].rearrange("p (m s) -> p m s", m=M2)
        y_ps = small[0:1, CHUNKS * P:(CHUNKS + 1) * P]

        eye_landed = sem("eye_landed")
        rowid_landed = sem("rowid_landed")
        weights_landed = sem("weights_landed")
        table_landed = [sem(f"table_landed{k}") for k in range(NP)]
        part_split = sem("part_split")
        part_taken = sem("part_taken")
        early_ids_landed = sem("early_ids_landed")
        late_ids_landed = sem("late_ids_landed")
        ids_cast = sem("ids_cast")
        onehot_ready = [sem(f"onehot_ready{k}") for k in range(NP)]
        picked_full = [sem(f"picked_full{b}") for b in range(2)]
        picked_kept = [sem(f"picked_kept{b}") for b in range(2)]
        placed = sem("placed")
        idx_landed = [sem(f"idx_landed{s}") for s in range(2)]
        dense_landed = [sem(f"dense_landed{s}") for s in range(2)]
        rows_landed = [[sem(f"rows_landed{s}_{g}") for g in range(NG)] for s in range(2)]
        rows_used = [sem(f"rows_used{s}") for s in range(2)]
        gathers_begun = sem("gathers_begun")
        w1d_summed = sem("w1d_summed")
        pads_zeroed = sem("pads_zeroed")
        turned_full = [sem(f"turned_full{b}") for b in range(2)]
        turned_kept = [sem(f"turned_kept{b}") for b in range(2)]
        gram_full = [sem(f"gram_full{b}") for b in range(2)]
        gram_kept = [sem(f"gram_kept{b}") for b in range(2)]
        dots_ready = sem("dots_ready")
        packed_ready = sem("packed_ready")
        pairs_full = sem("pairs_full")
        pairs_kept = sem("pairs_kept")
        pre1_full = sem("pre1_full")
        h1_ready = sem("h1_ready")
        pre2_full = sem("pre2_full")
        h2_ready = sem("h2_ready")
        y_full = sem("y_full")
        y_kept = sem("y_kept")
        stored = sem("stored")

        WEIGHT_DMAS = 6
        PICK_USES = [(NP + 1) // 2, NP // 2]
        LATE = NP - EARLY

        def load_picked_ids(eng, first, last, r, landed):
            src = picked_ids[first:last, r, :]
            src = bass.AP(tensor=src.tensor, offset=src.offset, ap=[[0, ROWS_PER_PART]] + [list(a) for a in src.ap])
            eng.dma_start(idb[:, first:last, :], src).then_inc(landed, 16)

        block = ctx.enter_context(nc.Block())

        @block.sync
        def _(sp):
            def load_tile(i, s):
                sp.wait_ge(rows_used[s], i + 1)
                sp.dma_start(idx[s][:, :], ids_v[:, i * 2 + s, :]).then_inc(idx_landed[s], 16)
                sp.dma_start(rows[s][:, DENSE, :], dense_v[:, i * 2 + s, :]).then_inc(dense_landed[s], 16)

            def load_table(k):
                src = tables[PICKED[k]].rearrange("(p c) d -> p c d", c=PARTS)
                sp.dma_start(left[k][:, :, :], src).then_inc(table_landed[k], 16)

            def round_(i, builds_early):
                sp.wait_ge(onehot_ready[NP - 1], i + 1)
                load_picked_ids(sp, EARLY, NP, i + 1, late_ids_landed)
                load_tile(i + 1, 0)
                load_tile(i + 1, 1)
                if builds_early:
                    sp.wait_ge(onehot_ready[EARLY - 1], i + 2)
                    load_picked_ids(sp, 0, EARLY, i + 2, early_ids_landed)

            load_tile(0, 0)
            load_table(0)
            sp.dma_start(rowid[:, :], row_of).then_inc(rowid_landed, 16)
            load_picked_ids(sp, 0, EARLY, 0, early_ids_landed)
            for k in range(1, NP):
                load_table(k)
            load_picked_ids(sp, EARLY, NP, 0, late_ids_landed)
            sp.dma_start(ident[:, :], eye).then_inc(eye_landed, 16)
            load_tile(0, 1)
            sp.dma_start(w1d2[:, :, :], w1_dense.rearrange("(a p) n -> p a n", a=2)).then_inc(weights_landed, 16)
            sp.dma_start(w1p[:, :, :], w1_pairs.rearrange("(c p) n -> p c n", c=CHUNKS)).then_inc(weights_landed, 16)
            sp.dma_start(w2s[:, :, :], w2.rearrange("(c p) n -> p c n", p=P)).then_inc(weights_landed, 16)
            with nc.allow_non_contiguous_dma(reason="a few hundred words, once"):
                sp.dma_start(b1s[:, :], b1.rearrange("(c p) -> p c", p=P)).then_inc(weights_landed, 16)
                sp.dma_start(b2s[:, :], b2.rearrange("(c p) -> p c", p=P)).then_inc(weights_landed, 16)
                sp.dma_start(w3s[:, :], w3.rearrange("(c p) o -> p (c o)", p=P)).then_inc(weights_landed, 16)
            sp.wait_ge(onehot_ready[EARLY - 1], 1)
            load_picked_ids(sp, 0, EARLY, 1, early_ids_landed)
            with sp.Fori(0, ROUNDS - 2) as i:
                round_(i, True)
            round_(ROUNDS - 2, False)
            sp.wait_ge(y_kept, TILES)
            sp.dma_start(out_v, y[:, :, :].rearrange("o p t -> o (p t)")).then_inc(stored, 16)
            sp.wait_ge(stored, 16)

        @block.gpsimd
        def _(pool):
            for free in (*rows_used, *turned_kept, *gram_kept, *picked_kept, dots_ready):
                pool.sem_inc(free, 1)
            with pool.Fori(0, ROUNDS) as i:
                for s in range(2):
                    pool.wait_ge(idx_landed[s], (i + 1) * 16)
                    pool.sem_inc(gathers_begun, 1)
                    for g, group in enumerate(GROUPS):
                        for v in group:
                            if v != DENSE:
                                f = ORDER[v]
                                pool.indirect_dma_start(
                                    rows[s][:, v, :], None, tables[f],
                                    bass.IndirectOffsetOnAxis(ap=idx[s][:, f:f + 1], axis=0),
                                ).then_inc(rows_landed[s][g], 16)

        def keep_turned(eng, copy, i, s, bank):
            for g, group in enumerate(GROUPS):
                r = s * NG + g
                if r % 2 == bank:
                    eng.wait_ge(turned_full[bank], i * NG + (r // 2 + 1))
                    dst = vecs[s][:, :, group[0]:group[-1] + 1].rearrange("p (q j) v -> p v j q", j=4)
                    src = turned[bank][:, 0:len(group), :].rearrange("p v (j q) -> p v j q", j=4)
                    copy(dst, src).then_inc(turned_kept[bank], 1)

        def keep_gram(eng, copy, i, s, quadrants):
            for n in range(FILLS):
                eng.wait_ge(gram_full[n % 2], i * FILLS + (s * FILLS // 2 + n // 2 + 1))
                if n == 0:
                    eng.wait_ge(dots_ready, i * 2 + (1 + s))
                for j in quadrants:
                    src = gram[n % 2][32 * j:32 * j + 32, 0:PER_FILL * 4 * VECS]
                    src = src.rearrange("p (q j v) -> p q j v", j=4, v=VECS)[:, :, j, :]
                    last = copy(blocks[32 * j:32 * j + 32, n * PER_FILL:(n + 1) * PER_FILL, :], src)
                last.then_inc(gram_kept[n % 2], 1)

        @block.scalar
        def _(act):
            for k, a in SPLIT_ORDER:
                if a == 0:
                    act.wait_ge(table_landed[k], 16)
                else:
                    act.wait_ge(part_taken, TAKEN_ORDER.index((k, a - 1)) + 1)
                nc.scalar.copy(parts[k][:, :, a, :], left[k][:, :, :]).then_inc(part_split, 1)

            def keep_picked(k, n):
                b = k % 2
                act.wait_ge(picked_full[b], n * PICK_USES[b] + (k // 2 + 1))
                if not (isinstance(n, int) and n == 0):
                    act.wait_ge(placed, n * 2)
                nc.scalar.copy(picks[:, k, :], picked[b][:, 0:WIDE]).then_inc(picked_kept[b], 1)

            def place(i, s):
                dst = vecs[s][:, :, DENSE + 1:VECS].rearrange("p (q j) v -> p v j q", j=4)
                src = picks[:, :, s * P:(s + 1) * P].rearrange("p v (j q) -> p v j q", j=4)
                nc.scalar.copy(dst, src).then_inc(placed, 1)

            def relu_h1(tiles):
                act.wait_ge(pre1_full, tiles + 1)
                for m in range(M1):
                    nc.scalar.activation(h1[:, m, :], pre1[:, m, :], ACT.Relu,
                                         bias=b1s[:, m:m + 1]).then_inc(h1_ready, 1)

            def relu_h2(tiles):
                act.wait_ge(pre2_full, tiles + 1)
                for m in range(M2):
                    nc.scalar.activation(h2[:, m, :], pre2[:, m, :], ACT.Relu,
                                         bias=b2s[:, m:m + 1]).then_inc(h2_ready, 1)

            def keep_y(tiles):
                act.wait_ge(y_full, tiles + 1)
                nc.scalar.copy(y[:, :, bass.ds(tiles, 1)],
                               y_ps.rearrange("o (p t) -> o p t", t=1)).then_inc(y_kept, 1)

            def round_(i, first, picks_next):
                def keep_complete(s, *gaps):
                    if picks_next:
                        for k in picks_complete(s, *gaps):
                            keep_picked(k, i + 1)

                for s in range(2):
                    has_last = s == 1 or not first
                    last_tile = i * 2 + (s - 1)
                    if has_last:
                        relu_h1(last_tile)
                    keep_turned(act, nc.scalar.copy, i, s, 1)
                    if has_last:
                        relu_h2(last_tile)
                    if s == 0:
                        for b in range(2):
                            act.wait_ge(picked_kept[b], i * PICK_USES[b] + (1 + PICK_USES[b]))
                        place(i, 0)
                    keep_gram(act, nc.scalar.copy, i, s, (0, 1))
                    if s == 0:
                        place(i, 1)
                    keep_complete(s, L1_GAP, TURN_GAP, PLACE_GAP)
                    if has_last:
                        keep_y(last_tile)
                    act.wait_ge(dots_ready, i * 2 + (1 + s + 1))
                    nc.scalar.copy(packed[:, :].rearrange("p (v k) -> p v k", k=SHIFTS),
                                   shifted).then_inc(packed_ready, 1)
                    keep_complete(s, GRAM_GAP)
                    act.wait_ge(pairs_full, i * 2 + (s + 1))
                    nc.scalar.copy(pairs[:, :, :], pairs_ps).then_inc(pairs_kept, 1)

            for k in range(NP):
                keep_picked(k, 0)
            act.wait_ge(weights_landed, 16 * WEIGHT_DMAS)
            round_(0, True, True)
            with act.Fori(1, ROUNDS - 1) as i:
                round_(i, False, True)
            round_(ROUNDS - 1, False, False)
            relu_h1(TILES - 1)
            relu_h2(TILES - 1)
            keep_y(TILES - 1)

        @block.vector
        def _(dve):
            for s in range(2):
                nc.vector.memset(vecs[s][:, :, VECS:SLOTS], 0.0).then_inc(pads_zeroed, 1)
            def take(k, a):
                dve.wait_ge(part_split, SPLIT_ORDER.index((k, a)) + 1)
                nc.vector.tensor_tensor(left[k][:, :, :], left[k][:, :, :], parts[k][:, :, a, :],
                                        ALU.subtract).then_inc(part_taken, 1)

            def build(k, n, landed, casts):
                dve.wait_ge(landed, n * 16 + 16)
                if not (isinstance(n, int) and n == 0):
                    b = k % 2
                    dve.wait_ge(picked_full[b], (n - 1) * PICK_USES[b] + (k // 2 + 1))
                nc.vector.tensor_copy(idh[:, k, :], idb[:, k, :]).then_inc(ids_cast, 1)
                dve.wait_ge(ids_cast, casts + 1)
                for c in range(PARTS):
                    last = nc.vector.tensor_scalar(onehot[k][:, c, :], idh[:, k, :], rowid[:, c:c + 1], None,
                                                   ALU.is_equal)
                last.then_inc(onehot_ready[k], 1)

            def round_(i, picks_next, builds_early):
                for s in range(2):
                    keep_turned(dve, nc.vector.tensor_copy, i, s, 0)
                    keep_gram(dve, nc.vector.tensor_copy, i, s, (2, 3))
                    for b in range(2):
                        dve.wait_ge(gram_kept[b], i * (2 * FILLS) + (1 + (s + 1) * FILLS))
                    by_vec = blocks[:, :, :].rearrange("p q v -> p v q")
                    nc.vector.transpose(dots[:, 0:VECS, :], by_vec)
                    nc.vector.transpose(dots[:, VECS:VECS + SHIFTS, :], by_vec[:, 0:SHIFTS, :]).then_inc(dots_ready, 1)
                    if s == 0 and picks_next:
                        for k in range(EARLY, NP):
                            build(k, i + 1, late_ids_landed, i * NP + (NP + EARLY + k - EARLY))
                    if s == 1 and builds_early:
                        for k in range(EARLY):
                            build(k, i + 2, early_ids_landed, i * NP + (NP + EARLY + LATE + k))

            dve.wait_ge(rowid_landed, 16)
            for k in range(NP):
                build(k, 0, early_ids_landed if k < EARLY else late_ids_landed, k)
                for at, step in enumerate(TAKEN_ORDER):
                    if at * NP // len(TAKEN_ORDER) == k:
                        take(*step)
            dve.wait_ge(weights_landed, 16 * WEIGHT_DMAS)
            nc.vector.tensor_tensor(w1d[:, :], w1d2[:, 0, :], w1d2[:, 1, :], ALU.add).then_inc(w1d_summed, 1)
            for k in range(EARLY):
                build(k, 1, early_ids_landed, NP + k)
            with dve.Fori(0, ROUNDS - 2) as i:
                round_(i, True, True)
            round_(ROUNDS - 2, True, False)
            round_(ROUNDS - 1, False, False)

        @block.tensor
        def _(pe):
            def pick(n, first, last):
                for at in range(first, last):
                    k, (a, c) = at // (PARTS * SPLIT), divmod(at % (PARTS * SPLIT), PARTS)
                    b = k % 2
                    begins, ends = at % (PARTS * SPLIT) == 0, (at + 1) % (PARTS * SPLIT) == 0
                    if begins:
                        pe.wait_ge(onehot_ready[k], n + 1)
                        pe.wait_ge(picked_kept[b], n * PICK_USES[b] + (1 + k // 2))
                    if c == 0 and isinstance(n, int) and n == 0:
                        pe.wait_ge(part_split, SPLIT_ORDER.index((k, a)) + 1)
                    product = nc.tensor.matmul(picked[b][:, 0:WIDE], parts[k][:, c, a, :], onehot[k][:, c, :],
                                               start=begins, stop=ends)
                    if ends:
                        product.then_inc(picked_full[b], 1)

            def layer1(tiles, s):
                pe.wait_ge(pairs_kept, tiles + 1)
                dense_t = vecs[s][:, :, DENSE].rearrange("p (q j) -> p j q", j=4)
                for m in range(M1):
                    nc.tensor.matmul(pre1[:, m, :], w1d[:, m * P:(m + 1) * P], dense_t,
                                     start=True, stop=False)
                    for c in range(CHUNKS):
                        last = nc.tensor.matmul(pre1[:, m, :], w1p[:, c, m * P:(m + 1) * P], pairs[:, c, :],
                                                start=False, stop=(c == CHUNKS - 1))
                last.then_inc(pre1_full, 1)

            def layer2(tiles):
                for m in range(M2):
                    for c in range(M1):
                        if m == 0:
                            pe.wait_ge(h1_ready, tiles * M1 + (c + 1))
                        last = nc.tensor.matmul(pre2[:, m, :], w2s[:, c, m * P:(m + 1) * P], h1[:, c, :],
                                                start=(c == 0), stop=(c == M1 - 1))
                last.then_inc(pre2_full, 1)

            def layer3(tiles):
                pe.wait_ge(h2_ready, tiles * M2 + M2)
                for c in range(M2):
                    last = nc.tensor.matmul(y_ps, w3s[:, c:c + 1], h2[:, c, :], start=(c == 0), stop=(c == M2 - 1))
                last.then_inc(y_full, 1)

            def round_(i, first, picks_next):
                for s in range(2):
                    has_last = s == 1 or not first
                    last_tile = i * 2 + (s - 1)

                    def gap(g):
                        if picks_next:
                            pick(i + 1, PICK_AT[s * GAPS + g], PICK_AT[s * GAPS + g + 1])

                    gap(L1_GAP)
                    if has_last:
                        layer1(last_tile, 1 - s)
                    for g, group in enumerate(GROUPS):
                        r = s * NG + g
                        n = sum(v != DENSE for v in group)
                        if n:
                            pe.wait_ge(rows_landed[s][g], i * (16 * n) + 16 * n)
                        if DENSE in group:
                            pe.wait_ge(dense_landed[s], i * 16 + 16)
                        pe.wait_ge(turned_kept[r % 2], i * NG + (1 + r // 2))
                        for k, v in enumerate(group):
                            last = nc.tensor.transpose(turned[r % 2][:, k, :], rows[s][:, v, :], ident[:, :])
                        last.then_inc(turned_full[r % 2], 1)
                        if g == TURN_GAP_AFTER:
                            gap(TURN_GAP)
                        if g == L2_AFTER and has_last:
                            layer2(last_tile)
                    gap(PLACE_GAP)
                    for b in range(2):
                        used = len([r for r in range((s + 1) * NG) if r % 2 == b])
                        pe.wait_ge(turned_kept[b], i * NG + (1 + used))
                    pe.wait_ge(placed, i * 2 + (s + 1))
                    four = vecs[s][:, :, :].rearrange("p (q j) v -> p q j v", j=4)
                    for n in range(FILLS):
                        pe.wait_ge(gram_kept[n % 2], i * (2 * FILLS) + (1 + s * FILLS + n // 2 * 2))
                        for k in range(PER_FILL):
                            q = n * PER_FILL + k
                            last = nc.tensor.matmul(
                                gram[n % 2][:, k * 4 * VECS:(k + 1) * 4 * VECS],
                                four[:, q, :, :].rearrange("p j v -> p (j v)"), four[:, q, :, 0:VECS],
                                start=True, stop=True)
                            if q == 0:
                                last.then_inc(rows_used[s], 1)
                        last.then_inc(gram_full[n % 2], 1)
                    if has_last:
                        layer3(last_tile)
                    gap(GRAM_GAP)
                    pe.wait_ge(packed_ready, i * 2 + (s + 1))
                    if has_last:
                        pe.wait_ge(y_kept, i * 2 + s)
                    for c in range(CHUNKS):
                        last = nc.tensor.transpose(pairs_ps[:, c, :], packed[:, c * CHUNK:(c + 1) * CHUNK], ident[:, :])
                    last.then_inc(pairs_full, 1)

            pick(0, 0, PICKS)
            pe.wait_ge(eye_landed, 16)
            pe.wait_ge(weights_landed, 16 * WEIGHT_DMAS)
            pe.wait_ge(w1d_summed, 1)
            pe.wait_ge(pads_zeroed, 2)
            round_(0, True, True)
            with pe.Fori(1, ROUNDS - 1) as i:
                round_(i, False, True)
            round_(ROUNDS - 1, False, False)
            layer1(TILES - 1, 1)
            layer2(TILES - 1)
            layer3(TILES - 1)




def kernel(**inputs):
    import numpy as _np
    import concourse.bacc as _bacc
    from concourse import mybir as _mybir
    from concourse.bass_utils import run_bass_kernel_spmd as _run

    x = {name: _np.asarray(a) for name, a in inputs.items()}
    w1 = x["W_top1"]
    given = {"dense": x["r_dense_features"], "ids": x["ids"]}
    given |= {f"table{f}": x[f"tbl_{f}"] for f in range(TABLES)}
    rounds = x["ids"].shape[0] // (2 * P)
    given["picked_ids"] = x["ids"][:, PICKED].reshape(P, rounds, 2, NP).transpose(3, 1, 2, 0).reshape(NP, rounds, 2 * P)
    given |= {"w1_pairs": w1[_np.array(pair_rows())],
              "w1_dense": _np.concatenate([w1[:P], w1[-P:]]),
              "b1": x["b_top1"], "w2": x["W_top2"], "b2": x["b_top2"], "w3": x["W_top3"],
              "eye": _np.eye(P, dtype=_np.float32),
              "row_of": _np.arange(ROWS, dtype=_np.float32).reshape(ROWS_PER_PART, PARTS)}
    nc = _bacc.Bacc("TRN2", target_bir_lowering=False, num_devices=1)
    aps, arrays = {}, {}
    for name, a in given.items():
        a = _np.ascontiguousarray(a)
        arrays[f"in_{name}"] = a
        aps[name] = nc.dram_tensor(f"in_{name}", a.shape, _mybir.dt.from_np(a.dtype), kind="ExternalInput").ap()
    out = nc.dram_tensor("out_y", (x["ids"].shape[0], 1), _mybir.dt.float32, kind="ExternalOutput").ap()
    dlrm_tower(nc, aps["dense"], aps["ids"], aps["picked_ids"], [aps[f"table{f}"] for f in range(TABLES)], aps["w1_pairs"],
               aps["w1_dense"], aps["b1"], aps["w2"], aps["b2"], aps["w3"], aps["eye"], aps["row_of"],
               out)
    r = _run(nc, [arrays], core_ids=[0])
    return r.results[0]["out_y"]
```

```python
import concourse.bass as bass
from concourse import mybir
from contextlib import ExitStack

F32 = mybir.dt.float32
BF16 = mybir.dt.bfloat16
F16 = mybir.dt.float16
I32 = mybir.dt.int32
ACT = mybir.ActivationFunctionType
ALU = mybir.AluOpType

P = 128
TABLES = 26
VECS = TABLES + 1
SLOTS = 32
SHIFTS = (VECS - 1) // 2
PAIRS = VECS * SHIFTS
VECS_PER_CHUNK = 9
CHUNKS = VECS // VECS_PER_CHUNK
CHUNK = VECS_PER_CHUNK * SHIFTS
QUADS = P // 4
STATIONARY = 3 * SLOTS + VECS
PER_FILL = 4
FILLS = QUADS // PER_FILL

PICKED = [25, 0, 7, 15, 16, 21]
HALF = 0
ROWS = 1000
PARTS = 8
ROWS_PER_PART = ROWS // PARTS
SPLIT = 3
GATHERED = [f for f in range(TABLES) if f not in PICKED]
DENSE = len(GATHERED)
ORDER = [*GATHERED, TABLES, *PICKED]
GROUP = 4
GROUPS = [list(range(g, min(g + GROUP, DENSE + 1))) for g in range(0, DENSE + 1, GROUP)]
NG = len(GROUPS)
NP = len(PICKED)
WIDTHS = [P if k == HALF else 2 * P for k in range(NP)]
PICK_USES = [(NP + 1) // 2, NP // 2]
EARLY = 3
SPLIT_ORDER = [*range(EARLY, NP), *range(EARLY)]
PICKS_MISSING = [(EARLY + 1) // 2, EARLY // 2]

FOLD_GROUPS, REST_GROUPS, FIRST_TURNED = (0, 1, 2, 3), (4, 5), (0, 1)

L1_GAP, TURN_GAP, PLACE_GAP, GRAM_GAP = range(4)
GAPS = 4
TURN_GAP_AFTER = 1
L2_AFTER = 3
PICKS = NP * PARTS * SPLIT
PICK_SHARES = [24, 8, 18, 28] + [10, 10, 19, 27]
PICK_AT = [sum(PICK_SHARES[:k]) for k in range(2 * GAPS + 1)]
PICK_AT_FIRST = [0, 0, PARTS * SPLIT, PARTS * SPLIT + PARTS, 2 * PARTS * SPLIT, 80, 96, 117, PICKS]


def pick_range(i, s, gap):
    at = PICK_AT_FIRST if isinstance(i, int) and i == 0 else PICK_AT
    return at[s * GAPS + gap], at[s * GAPS + gap + 1]


def picks_complete(i, s, *gaps):
    per_table = PARTS * SPLIT
    return [k for gap in gaps for k in range(NP)
            if pick_range(i, s, gap)[0] < (k + 1) * per_table <= pick_range(i, s, gap)[1]]


def onehots_built(k, n):
    return n if k < EARLY else n + 1


def picks_done(k, n):
    return n * PICK_USES[k % 2] + (k // 2 + 1 - PICKS_MISSING[k % 2])


def picked_but_gathered(i, s):
    if isinstance(i, int) and i == 0:
        return EARLY
    return HALF + 1 if s == 0 else 0


def groups_of(i, s):
    return [*GROUPS[:-1], [*GROUPS[-1], *range(DENSE + 1, DENSE + 1 + picked_but_gathered(i, s))]]


def pair_rows():
    rows = []
    for v in range(VECS):
        for k in range(1, SHIFTS + 1):
            a, b = sorted((ORDER[v], ORDER[(v + k) % VECS]))
            if b == TABLES:
                rows.append(P + a)
            else:
                rows.append(P + TABLES + a * TABLES - a * (a + 1) // 2 + b - a - 1)
    return rows


def dlrm_tower(nc, dense, ids, picked_ids, tables, w1_pairs, w1_dense, b1, w2, b2, w3, eye, row_of, out):
    B = dense.shape[0]
    TILES = B // P
    ROUNDS = TILES // 2
    WIDE = 2 * P
    H1, H2 = w2.shape
    M1 = H1 // P

    dense_v = dense.rearrange("(p t) d -> p t d", t=TILES)
    ids_v = ids.rearrange("(p t) f -> p t f", t=TILES)
    out_v = out.rearrange("(p t) o -> p (t o)", t=TILES)

    ctx = ExitStack()
    with ctx:
        def sb(name, shape, dt=F32):
            return ctx.enter_context(nc.sbuf_tensor(name, shape, dt))

        def pb(name, shape):
            return ctx.enter_context(nc.psum_tensor(name, shape, F32))

        def sem(name):
            return ctx.enter_context(nc.semaphore(name))

        ident = sb("ident", [P, P])
        rowid = sb("rowid", [ROWS_PER_PART, PARTS])
        w1p = sb("w1p", [CHUNK, CHUNKS, H1])
        w1d2 = sb("w1d2", [P, 2, H1])
        w1d = sb("w1d", [P, H1])
        w2s = sb("w2s", [P, M1, H2])
        b1s = sb("b1s", [P, M1])
        b2s = sb("b2s", [P, H2])
        w3s = sb("w3s", [P, H2])
        idx = [sb(f"idx{s}", [P, TABLES], I32) for s in range(2)]
        rows = [sb(f"rows{s}", [P, DENSE + 1 + EARLY, P]) for s in range(2)]
        vecs = [sb(f"vecs{s}", [P, P, SLOTS]) for s in range(2)]
        blocks = sb("blocks", [P, QUADS, VECS])
        dots = sb("dots", [P, VECS + SHIFTS, SLOTS])
        packed = sb("packed", [P, PAIRS])
        pairs = sb("pairs", [CHUNK, CHUNKS, P])
        h1 = sb("h1", [P, M1, P])
        z2 = sb("z2", [P, H2])
        weighted = sb("weighted", [P, H2])
        y = sb("y", [P, TILES])
        idb = sb("idb", [ROWS_PER_PART, NP, WIDE], I32)
        idh = sb("idh", [ROWS_PER_PART, NP, WIDE], F16)
        onehot = [sb(f"onehot{k}", [ROWS_PER_PART, PARTS, WIDTHS[k]], BF16) for k in range(NP)]
        parts = [sb(f"parts{k}", [ROWS_PER_PART, PARTS, SPLIT, P], BF16) for k in range(NP)]
        picks = sb("picks", [P, NP, WIDE])
        table = [sb(f"table{k}", [ROWS_PER_PART, PARTS, P]) for k in range(NP)]
        rest = [sb(f"rest{k}", [ROWS_PER_PART, PARTS, P]) for k in range(2)]

        def shifted_of(first, last):
            flat = dots[:, :, :].rearrange("p a b -> p (a b)")
            return bass.AP(tensor=flat.tensor, offset=flat.offset + SLOTS + first * (SLOTS + 1),
                           ap=[list(flat.ap[0]), [SLOTS + 1, last - first], [SLOTS, SHIFTS]])

        turned = [pb(f"turned{b}", [P, GROUP, P]) for b in range(2)]
        gram = [pb(f"gram{b}", [P, 512]) for b in range(2)]
        picked = [pb(f"picked{b}", [P, 512]) for b in range(2)]
        small = pb("small", [P, 512])
        pre1 = pb("pre1", [P, M1, P])
        pairs_ps = small[0:CHUNK, 0:CHUNKS * P].rearrange("p (c s) -> p c s", c=CHUNKS)
        pre2 = small[:, 0:H2]
        final_pairs = [gram[1][0:CHUNK, 0:P], gram[0][0:CHUNK, 0:(CHUNKS - 1) * P]]
        final_pre1 = [pre1[:, 0, :], picked[0][:, 0:P], picked[1][:, 0:P], turned[1][:, 0, :]]

        eye_landed = sem("eye_landed")
        rowid_landed = sem("rowid_landed")
        weights_landed = sem("weights_landed")
        table_landed = [sem(f"table_landed{k}") for k in range(NP)]
        first_kept = sem("first_kept")
        second_kept = sem("second_kept")
        rest_left = sem("rest_left")
        last_kept = sem("last_kept")
        early_ids_landed = sem("early_ids_landed")
        late_ids_landed = sem("late_ids_landed")
        ids_cast = sem("ids_cast")
        onehot_ready = [sem(f"onehot_ready{k}") for k in range(NP)]
        picked_full = [sem(f"picked_full{b}") for b in range(2)]
        picked_kept = [sem(f"picked_kept{b}") for b in range(2)]
        placed = sem("placed")
        idx_landed = [sem(f"idx_landed{s}") for s in range(2)]
        dense_landed = [sem(f"dense_landed{s}") for s in range(2)]
        rows_landed = [[sem(f"rows_landed{s}_{g}") for g in range(NG)] for s in range(2)]
        extra_landed = [sem(f"extra_landed{s}") for s in range(2)]
        rows_used = [sem(f"rows_used{s}") for s in range(2)]
        gathers_begun = sem("gathers_begun")
        w1d_summed = sem("w1d_summed")
        pads_zeroed = sem("pads_zeroed")
        blocks_zeroed = sem("blocks_zeroed")
        turned_full = [sem(f"turned_full{b}") for b in range(2)]
        turned_kept = [sem(f"turned_kept{b}") for b in range(2)]
        gram_full = [sem(f"gram_full{b}") for b in range(2)]
        gram_kept = [sem(f"gram_kept{b}") for b in range(2)]
        dots_ready = sem("dots_ready")
        packed_ready = sem("packed_ready")
        pairs_full = sem("pairs_full")
        pairs_kept = sem("pairs_kept")
        pre1_full = sem("pre1_full")
        h1_ready = sem("h1_ready")
        pre2_full = sem("pre2_full")
        z2_ready = sem("z2_ready")
        y_ready = sem("y_ready")
        stored = sem("stored")

        WEIGHT_DMAS = 6
        LATE = NP - EARLY

        def upper_half(t):
            return t[:, :, :].bitcast(BF16).rearrange("p c (d h) -> p c d h", h=2)[:, :, :, 1]

        def load_picked_ids(eng, first, last, r, landed):
            src = picked_ids[first:last, r, :]
            src = bass.AP(tensor=src.tensor, offset=src.offset, ap=[[0, ROWS_PER_PART]] + [list(a) for a in src.ap])
            eng.dma_start(idb[:, first:last, :], src).then_inc(landed, 16)

        def on_all(v):
            return bass.AP(tensor=v.tensor, offset=v.offset, ap=[[0, P], list(v.ap[0])])

        block = ctx.enter_context(nc.Block())

        @block.sync
        def _(sp):
            def load_tile(i, s):
                sp.wait_ge(rows_used[s], i + 1)
                sp.dma_start(idx[s][:, :], ids_v[:, i * 2 + s, :]).then_inc(idx_landed[s], 16)
                sp.dma_start(rows[s][:, DENSE, :], dense_v[:, i * 2 + s, :]).then_inc(dense_landed[s], 16)

            def load_table(k):
                src = tables[PICKED[k]].rearrange("(p c) d -> p c d", c=PARTS)
                sp.dma_start(table[k][:, :, :], src).then_inc(table_landed[k], 16)

            def round_(i, builds_early):
                sp.wait_ge(onehot_ready[NP - 1], onehots_built(NP - 1, i))
                load_picked_ids(sp, EARLY, NP, i + 1, late_ids_landed)
                if builds_early:
                    sp.wait_ge(onehot_ready[EARLY - 1], onehots_built(EARLY - 1, i + 1))
                    load_picked_ids(sp, 0, EARLY, i + 2, early_ids_landed)
                load_tile(i + 1, 0)
                load_tile(i + 1, 1)

            load_tile(0, 0)
            load_table(SPLIT_ORDER[0])
            sp.dma_start(rowid[:, :], row_of).then_inc(rowid_landed, 16)
            load_picked_ids(sp, EARLY, NP, 0, late_ids_landed)
            load_table(SPLIT_ORDER[1])
            load_table(SPLIT_ORDER[2])
            sp.dma_start(ident[:, :], eye).then_inc(eye_landed, 16)
            load_picked_ids(sp, 0, EARLY, 1, early_ids_landed)
            load_table(SPLIT_ORDER[3])
            load_table(SPLIT_ORDER[4])
            load_tile(0, 1)
            sp.wait_ge(extra_landed[0], 16 * EARLY)
            for k in SPLIT_ORDER[5:]:
                load_table(k)
            sp.dma_start(w1d2[:, :, :], w1_dense.rearrange("(a p) n -> p a n", a=2)).then_inc(weights_landed, 16)
            sp.dma_start(w1p[:, :, :], w1_pairs.rearrange("(c p) n -> p c n", c=CHUNKS)).then_inc(weights_landed, 16)
            sp.dma_start(w2s[:, :, :], w2.rearrange("(c p) n -> p c n", p=P)).then_inc(weights_landed, 16)
            with nc.allow_non_contiguous_dma(reason="a few hundred words, once"):
                sp.dma_start(b1s[:, :], b1.rearrange("(c p) -> p c", p=P)).then_inc(weights_landed, 16)
            sp.dma_start(b2s[:, :], on_all(b2)).then_inc(weights_landed, 16)
            sp.dma_start(w3s[:, :], on_all(w3.rearrange("n o -> (n o)"))).then_inc(weights_landed, 16)
            with sp.Fori(0, ROUNDS - 2) as i:
                round_(i, True)
            round_(ROUNDS - 2, False)
            sp.wait_ge(y_ready, TILES)
            sp.dma_start(out_v, y[:, :]).then_inc(stored, 16)
            sp.wait_ge(stored, 16)

        @block.gpsimd
        def _(pool):
            for free in (*rows_used, *turned_kept, *gram_kept, *picked_kept, dots_ready):
                pool.sem_inc(free, 1)

            def round_(i):
                for s in range(2):
                    pool.wait_ge(idx_landed[s], (i + 1) * 16)
                    pool.sem_inc(gathers_begun, 1)
                    for g, group in enumerate(GROUPS):
                        for v in group:
                            if v != DENSE:
                                f = ORDER[v]
                                pool.indirect_dma_start(
                                    rows[s][:, v, :], None, tables[f],
                                    bass.IndirectOffsetOnAxis(ap=idx[s][:, f:f + 1], axis=0),
                                ).then_inc(rows_landed[s][g], 16)
                    for v in groups_of(i, s)[-1][len(GROUPS[-1]):]:
                        f = ORDER[v]
                        pool.indirect_dma_start(
                            rows[s][:, v, :], None, tables[f],
                            bass.IndirectOffsetOnAxis(ap=idx[s][:, f:f + 1], axis=0),
                        ).then_inc(extra_landed[s], 16)

            round_(0)
            with pool.Fori(1, ROUNDS) as i:
                round_(i)

        def keep_turned(eng, copy, i, s, bank, groups=range(NG)):
            for g, group in enumerate(groups_of(i, s)):
                r = s * NG + g
                if r % 2 == bank and g in groups:
                    eng.wait_ge(turned_full[bank], i * NG + (r // 2 + 1))
                    dst = vecs[s][:, :, group[0]:group[-1] + 1].rearrange("p (q j) v -> p v j q", j=4)
                    src = turned[bank][:, 0:len(group), :].rearrange("p v (j q) -> p v j q", j=4)
                    copy(dst, src).then_inc(turned_kept[bank], 1)

        def keep_gram(eng, copy, i, s, quadrants):
            for n in range(FILLS):
                eng.wait_ge(gram_full[n % 2], i * FILLS + (s * FILLS // 2 + n // 2 + 1))
                if n == 0:
                    eng.wait_ge(dots_ready, i * 2 + (1 + s))
                for j in quadrants:
                    src = gram[n % 2][32 * j:32 * j + VECS, 0:PER_FILL * 4 * VECS]
                    src = src.rearrange("p (q j v) -> p q j v", j=4, v=VECS)[:, :, j, :]
                    last = copy(blocks[32 * j:32 * j + VECS, n * PER_FILL:(n + 1) * PER_FILL, :], src)
                last.then_inc(gram_kept[n % 2], 1)

        @block.scalar
        def _(act):
            def split_first(at):
                k = SPLIT_ORDER[at]
                act.wait_ge(table_landed[k], 16)
                nc.scalar.copy(parts[k][:, :, 0, :], upper_half(table[k])).then_inc(first_kept, 1)

            def split_second(at):
                k = SPLIT_ORDER[at]
                act.wait_ge(rest_left, at + 1)
                nc.scalar.copy(parts[k][:, :, 1, :], upper_half(rest[at % 2])).then_inc(second_kept, 1)

            def keep_picked(k, n):
                b = k % 2
                act.wait_ge(picked_full[b], picks_done(k, n))
                if not (isinstance(n, int) and n == 0):
                    act.wait_ge(placed, n * 2)
                nc.scalar.copy(picks[:, k, WIDE - WIDTHS[k]:WIDE],
                               picked[b][:, 0:WIDTHS[k]]).then_inc(picked_kept[b], 1)

            def place(i, s):
                first = picked_but_gathered(i, s)
                dst = vecs[s][:, :, DENSE + 1 + first:VECS].rearrange("p (q j) v -> p v j q", j=4)
                src = picks[:, first:NP, s * P:(s + 1) * P].rearrange("p v (j q) -> p v j q", j=4)
                nc.scalar.copy(dst, src).then_inc(placed, 1)

            def relu_h1(tiles):
                act.wait_ge(pre1_full, tiles + 1)
                for m in range(M1):
                    nc.scalar.activation(h1[:, m, :], pre1[:, m, :], ACT.Relu,
                                         bias=b1s[:, m:m + 1]).then_inc(h1_ready, 1)

            def keep_complete(i, s, *gaps):
                for k in picks_complete(i, s, *gaps):
                    keep_picked(k, i + 1)

            def pack(i, s):
                act.wait_ge(dots_ready, i * 2 + (1 + s + 1))
                nc.scalar.copy(packed[:, :].rearrange("p (v k) -> p v k", k=SHIFTS),
                               shifted_of(0, VECS)).then_inc(packed_ready, 1)

            def keep_pairs(i, s):
                act.wait_ge(pairs_full, i * 2 + (s + 1))
                nc.scalar.copy(pairs[:, :, :], pairs_ps).then_inc(pairs_kept, 1)

            def slot(i, s, picks_next, turns_last=False):
                relu_h1(i * 2 + (s - 1))
                keep_turned(act, nc.scalar.copy, i, s, 1, range(0, 2))
                if s == 0:
                    for b in range(2):
                        act.wait_ge(picked_kept[b], i * PICK_USES[b] + (1 + PICK_USES[b] - PICKS_MISSING[b]))
                    place(i, 0)
                keep_turned(act, nc.scalar.copy, i, s, 1, range(2, 4))
                if s == 0:
                    place(i, 1)
                if picks_next:
                    keep_complete(i, s, L1_GAP)
                keep_turned(act, nc.scalar.copy, i, s, 1, range(4, NG))
                if picks_next:
                    keep_complete(i, s, TURN_GAP)
                keep_gram(act, nc.scalar.copy, i, s, (0, 1))
                if turns_last:
                    keep_turned(act, nc.scalar.copy, i, 1, 1, FIRST_TURNED)
                if picks_next:
                    keep_complete(i, s, PLACE_GAP)
                pack(i, s)
                if picks_next:
                    keep_complete(i, s, GRAM_GAP)
                keep_pairs(i, s)

            def first_slot():
                for at in range(LATE):
                    split_first(at)
                    split_second(at)
                    if 1 <= at:
                        keep_picked(SPLIT_ORDER[at - 1], 0)
                keep_turned(act, nc.scalar.copy, 0, 0, 1, (1,))
                split_first(LATE)
                keep_picked(SPLIT_ORDER[LATE - 1], 0)
                split_first(LATE + 1)
                split_second(LATE)
                keep_turned(act, nc.scalar.copy, 0, 0, 1, range(2, NG - 1))
                for b in range(2):
                    act.wait_ge(picked_kept[b], 1 + PICK_USES[b] - PICKS_MISSING[b])
                place(0, 0)
                keep_turned(act, nc.scalar.copy, 0, 0, 1, (NG - 1,))
                act.wait_ge(blocks_zeroed, 1)
                split_second(LATE + 1)
                keep_gram(act, nc.scalar.copy, 0, 0, (0, 1))
                place(0, 1)
                keep_complete(0, 0, TURN_GAP)
                pack(0, 0)
                keep_complete(0, 0, GRAM_GAP)
                keep_pairs(0, 0)
                split_first(LATE + 2)
                split_second(LATE + 2)
                act.wait_ge(weights_landed, 16 * WEIGHT_DMAS)

            def last_slot(i):
                keep_turned(act, nc.scalar.copy, i, 1, 1, range(2, NG))
                relu_h1(TILES - 2)
                keep_gram(act, nc.scalar.copy, i, 1, (0, 1))
                act.wait_ge(dots_ready, TILES + 1)
                by_vec = packed[:, :].rearrange("p (v k) -> p v k", k=SHIFTS)
                nc.scalar.copy(by_vec[:, 0:VECS_PER_CHUNK, :], shifted_of(0, VECS_PER_CHUNK)).then_inc(packed_ready, 1)
                act.wait_ge(dots_ready, TILES + 2)
                nc.scalar.copy(by_vec[:, VECS_PER_CHUNK:VECS, :],
                               shifted_of(VECS_PER_CHUNK, VECS)).then_inc(packed_ready, 1)
                act.wait_ge(pairs_full, TILES)
                nc.scalar.copy(pairs[:, 0, :], final_pairs[0]).then_inc(pairs_kept, 1)
                act.wait_ge(pairs_full, TILES + 1)
                nc.scalar.copy(pairs[:, 1:CHUNKS, :],
                               final_pairs[1].rearrange("p (c s) -> p c s", s=P)).then_inc(pairs_kept, 1)
                act.wait_ge(pre2_full, TILES - 1)
                for m in range(M1):
                    act.wait_ge(pre1_full, TILES - 1 + (m + 1))
                    nc.scalar.activation(h1[:, m, :], final_pre1[m], ACT.Relu,
                                         bias=b1s[:, m:m + 1]).then_inc(h1_ready, 1)

            first_slot()
            slot(0, 1, True)
            with act.Fori(1, ROUNDS - 1) as i:
                for s in range(2):
                    slot(i, s, True)
            slot(ROUNDS - 1, 0, False, turns_last=True)
            last_slot(ROUNDS - 1)

        @block.vector
        def _(dve):
            for s in range(2):
                nc.vector.memset(vecs[s][:, :, VECS:SLOTS], 0.0).then_inc(pads_zeroed, 1)
            nc.vector.memset(blocks[:, :, :], 0.0).then_inc(blocks_zeroed, 1)

            def split(at):
                k = SPLIT_ORDER[at]
                dve.wait_ge(table_landed[k], 16)
                if at >= 2:
                    dve.wait_ge(second_kept, at - 1)
                    dve.wait_ge(last_kept, at - 1)
                nc.vector.tensor_tensor(rest[at % 2][:, :, :], table[k][:, :, :], upper_half(table[k]),
                                        ALU.subtract).then_inc(rest_left, 1)
                dve.wait_ge(rest_left, at + 1)
                nc.vector.tensor_tensor(parts[k][:, :, 2, :], rest[at % 2][:, :, :], upper_half(rest[at % 2]),
                                        ALU.subtract).then_inc(last_kept, 1)

            def build(k, n, landed, casts):
                dve.wait_ge(landed, onehots_built(k, n) * 16)
                if not (isinstance(n, int) and n == (1 if k < EARLY else 0)):
                    dve.wait_ge(picked_full[k % 2], picks_done(k, n - 1))
                picked_for = slice(WIDE - WIDTHS[k], WIDE)
                nc.vector.tensor_copy(idh[:, k, picked_for], idb[:, k, picked_for]).then_inc(ids_cast, 1)
                dve.wait_ge(ids_cast, casts + 1)
                for c in range(PARTS):
                    last = nc.vector.tensor_scalar(onehot[k][:, c, :], idh[:, k, picked_for], rowid[:, c:c + 1], None,
                                                   ALU.is_equal)
                last.then_inc(onehot_ready[k], 1)

            def builds(i, s, first, last, picks_next, builds_early):
                if s == 0 and picks_next:
                    for k in range(EARLY + first, EARLY + last):
                        build(k, i + 1, late_ids_landed, i * NP + (NP + k - EARLY))
                if s == 1 and builds_early:
                    for k in range(first, last):
                        build(k, i + 2, early_ids_landed, i * NP + (NP + LATE + k))

            by_vec = blocks[:, :, :].rearrange("p q v -> p v q")

            def keep_blocks(i, s):
                keep_gram(dve, nc.vector.tensor_copy, i, s, (2, 3))
                for b in range(2):
                    dve.wait_ge(gram_kept[b], i * (2 * FILLS) + (1 + (s + 1) * FILLS))

            def fold():
                nc.vector.transpose(dots[:, 0:VECS, :], by_vec)
                nc.vector.transpose(dots[:, VECS:VECS + SHIFTS, :], by_vec[:, 0:SHIFTS, :]).then_inc(dots_ready, 1)

            def layer3(tiles):
                dve.wait_ge(pre2_full, tiles + 1)
                if not (isinstance(tiles, int) and tiles == 0):
                    dve.wait_ge(y_ready, tiles)
                nc.vector.tensor_tensor(z2[:, :], pre2, b2s[:, :], ALU.add).then_inc(z2_ready, 1)
                dve.wait_ge(z2_ready, tiles + 1)
                nc.vector.scalar_tensor_tensor(weighted[:, :], z2[:, :], 0.0, w3s[:, :], ALU.max, ALU.mult,
                                               accum_out=y[:, bass.ds(tiles, 1)]).then_inc(y_ready, 1)

            def slot(i, s, picks_next, builds_early, turns_last=False):
                keep_turned(dve, nc.vector.tensor_copy, i, s, 0, (0,))
                builds(i, s, 0, 1, picks_next, builds_early)
                keep_turned(dve, nc.vector.tensor_copy, i, s, 0, range(1, NG))
                layer3(i * 2 + (s - 1))
                keep_blocks(i, s)
                if turns_last:
                    keep_turned(dve, nc.vector.tensor_copy, i, 1, 0, FIRST_TURNED)
                fold()
                builds(i, s, 1, LATE if s == 0 else EARLY, picks_next, builds_early)

            def first_slot():
                for at, k in enumerate(SPLIT_ORDER[:LATE]):
                    build(k, 0, late_ids_landed, at)
                    split(at)
                keep_turned(dve, nc.vector.tensor_copy, 0, 0, 0, (0,))
                build(0, 1, early_ids_landed, LATE)
                keep_turned(dve, nc.vector.tensor_copy, 0, 0, 0, (2,))
                split(LATE)
                build(1, 1, early_ids_landed, LATE + 1)
                keep_turned(dve, nc.vector.tensor_copy, 0, 0, 0, range(4, NG))
                split(LATE + 1)
                dve.wait_ge(blocks_zeroed, 1)
                keep_blocks(0, 0)
                fold()
                dve.wait_ge(weights_landed, 16 * WEIGHT_DMAS)
                nc.vector.tensor_tensor(w1d[:, :], w1d2[:, 0, :], w1d2[:, 1, :], ALU.add).then_inc(w1d_summed, 1)
                build(2, 1, early_ids_landed, LATE + 2)
                split(LATE + 2)
                builds(0, 0, 0, LATE, True, True)

            def last_slot(i):
                keep_turned(dve, nc.vector.tensor_copy, i, 1, 0, range(2, NG))
                keep_blocks(i, 1)
                first = VECS_PER_CHUNK + SHIFTS
                nc.vector.transpose(dots[:, 0:first, :], by_vec[:, 0:first, :]).then_inc(dots_ready, 1)
                nc.vector.transpose(dots[:, first:VECS, :], by_vec[:, first:VECS, :])
                nc.vector.transpose(dots[:, VECS:VECS + SHIFTS, :], by_vec[:, 0:SHIFTS, :]).then_inc(dots_ready, 1)
                layer3(TILES - 2)
                layer3(TILES - 1)

            dve.wait_ge(rowid_landed, 16)
            first_slot()
            slot(0, 1, True, True)
            with dve.Fori(1, ROUNDS - 2) as i:
                for s in range(2):
                    slot(i, s, True, True)
            for s in range(2):
                slot(ROUNDS - 2, s, True, False)
            slot(ROUNDS - 1, 0, False, False, turns_last=True)
            last_slot(ROUNDS - 1)

        @block.tensor
        def _(pe):
            def pick(n, first, last):
                for at in range(first, last):
                    k, (a, c) = at // (PARTS * SPLIT), divmod(at % (PARTS * SPLIT), PARTS)
                    b = k % 2
                    begins, ends = at % (PARTS * SPLIT) == 0, (at + 1) % (PARTS * SPLIT) == 0
                    if begins:
                        pe.wait_ge(onehot_ready[k], onehots_built(k, n))
                        pe.wait_ge(picked_kept[b], picks_done(k, n))
                    if c == 0 and isinstance(n, int) and n == (1 if k < EARLY else 0):
                        pe.wait_ge((first_kept, second_kept, last_kept)[a], SPLIT_ORDER.index(k) + 1)
                    product = nc.tensor.matmul(picked[b][:, 0:WIDTHS[k]], parts[k][:, c, a, :], onehot[k][:, c, :],
                                               start=begins, stop=ends)
                    if ends:
                        product.then_inc(picked_full[b], 1)

            def layer1(tiles, s, blocks_of_h1=range(M1)):
                pe.wait_ge(pairs_kept, tiles + 1)
                dense_t = vecs[s][:, :, DENSE].rearrange("p (q j) -> p j q", j=4)
                for m in blocks_of_h1:
                    nc.tensor.matmul(pre1[:, m, :], w1d[:, m * P:(m + 1) * P], dense_t,
                                     start=True, stop=False)
                    for c in range(CHUNKS):
                        last = nc.tensor.matmul(pre1[:, m, :], w1p[:, c, m * P:(m + 1) * P], pairs[:, c, :],
                                                start=False, stop=(c == CHUNKS - 1))
                if M1 - 1 in blocks_of_h1:
                    last.then_inc(pre1_full, 1)

            def layer2(tiles):
                for c in range(M1):
                    pe.wait_ge(h1_ready, tiles * M1 + (c + 1))
                    last = nc.tensor.matmul(pre2, h1[:, c, :], w2s[:, c, :], start=(c == 0), stop=(c == M1 - 1))
                last.then_inc(pre2_full, 1)

            def turn(i, s, groups=range(NG)):
                for g in groups:
                    group = groups_of(i, s)[g]
                    r = s * NG + g
                    n = sum(v != DENSE for v in GROUPS[g])
                    if n:
                        pe.wait_ge(rows_landed[s][g], i * (16 * n) + 16 * n)
                    if len(group) > len(GROUPS[g]):
                        pe.wait_ge(extra_landed[s], i * 16 + 16 * EARLY)
                    if DENSE in group:
                        pe.wait_ge(dense_landed[s], i * 16 + 16)
                    pe.wait_ge(turned_kept[r % 2], i * NG + (1 + r // 2))
                    for k, v in enumerate(group):
                        last = nc.tensor.transpose(turned[r % 2][:, k, :], rows[s][:, v, :], ident[:, :])
                    last.then_inc(turned_full[r % 2], 1)

            def grams(i, s):
                for b in range(2):
                    used = len([r for r in range((s + 1) * NG) if r % 2 == b])
                    pe.wait_ge(turned_kept[b], i * NG + (1 + used))
                pe.wait_ge(placed, i * 2 + (s + 1))
                four = vecs[s][:, :, :].rearrange("p (q j) v -> p q j v", j=4)
                for n in range(FILLS):
                    pe.wait_ge(gram_kept[n % 2], i * (2 * FILLS) + (1 + s * FILLS + n // 2 * 2))
                    for k in range(PER_FILL):
                        q = n * PER_FILL + k
                        last = nc.tensor.matmul(
                            gram[n % 2][0:STATIONARY, k * 4 * VECS:(k + 1) * 4 * VECS],
                            four[:, q, :, :].rearrange("p j v -> p (j v)")[:, 0:STATIONARY],
                            four[:, q, :, 0:VECS],
                            start=True, stop=True)
                        if q == 0:
                            last.then_inc(rows_used[s], 1)
                    last.then_inc(gram_full[n % 2], 1)

            def turn_pairs(i, s):
                pe.wait_ge(packed_ready, i * 2 + (s + 1))
                if s == 1 or not isinstance(i, int) or i > 0:
                    pe.wait_ge(z2_ready, i * 2 + s)
                for c in range(CHUNKS):
                    last = nc.tensor.transpose(pairs_ps[:, c, :], packed[:, c * CHUNK:(c + 1) * CHUNK], ident[:, :])
                last.then_inc(pairs_full, 1)

            def gap(i, s, g):
                pick(i + 1, *pick_range(i, s, g))

            def slot(i, s, picks_next, turns_last=False):
                last_tile = i * 2 + (s - 1)
                first = isinstance(i, int) and i == 0
                if picks_next and not first:
                    gap(i, s, L1_GAP)
                layer1(last_tile, 1 - s)
                if picks_next and first:
                    gap(i, s, L1_GAP)
                turn(i, s, range(TURN_GAP_AFTER + 1))
                if picks_next:
                    gap(i, s, TURN_GAP)
                turn(i, s, range(TURN_GAP_AFTER + 1, L2_AFTER + 1))
                layer2(last_tile)
                turn(i, s, range(L2_AFTER + 1, NG))
                if picks_next:
                    gap(i, s, PLACE_GAP)
                grams(i, s)
                if picks_next:
                    gap(i, s, GRAM_GAP)
                if turns_last:
                    turn(i, 1, FOLD_GROUPS)
                turn_pairs(i, s)

            def first_slot():
                pick(0, EARLY * PARTS * SPLIT, (NP - 1) * PARTS * SPLIT)
                pe.wait_ge(eye_landed, 16)
                turn(0, 0, (0,))
                pick(0, (NP - 1) * PARTS * SPLIT, PICKS)
                turn(0, 0, (1, 2))
                gap(0, 0, TURN_GAP)
                turn(0, 0, range(3, NG - 1))
                gap(0, 0, PLACE_GAP)
                turn(0, 0, (NG - 1,))
                pe.wait_ge(pads_zeroed, 2)
                grams(0, 0)
                gap(0, 0, GRAM_GAP)
                turn_pairs(0, 0)
                pe.wait_ge(weights_landed, 16 * WEIGHT_DMAS)
                pe.wait_ge(w1d_summed, 1)

            def last_slot(i):
                layer1(TILES - 2, 0, range(M1 // 2))
                turn(i, 1, REST_GROUPS)
                layer1(TILES - 2, 0, range(M1 // 2, M1))
                grams(i, 1)
                pe.wait_ge(h1_ready, (TILES - 1) * M1)
                dense_t = vecs[1][:, :, DENSE].rearrange("p (q j) -> p j q", j=4)
                for m in range(M1):
                    nc.tensor.matmul(final_pre1[m], w1d[:, m * P:(m + 1) * P], dense_t, start=True, stop=False)
                layer2(TILES - 2)
                pe.wait_ge(packed_ready, TILES)
                nc.tensor.transpose(final_pairs[0], packed[:, 0:CHUNK], ident[:, :]).then_inc(pairs_full, 1)
                pe.wait_ge(packed_ready, TILES + 1)
                for c in range(1, CHUNKS):
                    last = nc.tensor.transpose(final_pairs[1][:, (c - 1) * P:c * P],
                                               packed[:, c * CHUNK:(c + 1) * CHUNK], ident[:, :])
                last.then_inc(pairs_full, 1)
                pe.wait_ge(pairs_kept, TILES)
                for m in range(M1):
                    nc.tensor.matmul(final_pre1[m], w1p[:, 0, m * P:(m + 1) * P], pairs[:, 0, :],
                                     start=False, stop=False)
                pe.wait_ge(pairs_kept, TILES + 1)
                for m in range(M1):
                    for c in range(1, CHUNKS):
                        last = nc.tensor.matmul(final_pre1[m], w1p[:, c, m * P:(m + 1) * P], pairs[:, c, :],
                                                start=False, stop=(c == CHUNKS - 1))
                    last.then_inc(pre1_full, 1)
                pe.wait_ge(z2_ready, TILES - 1)
                layer2(TILES - 1)

            first_slot()
            slot(0, 1, True)
            with pe.Fori(1, ROUNDS - 1) as i:
                for s in range(2):
                    slot(i, s, True)
            slot(ROUNDS - 1, 0, False, turns_last=True)
            last_slot(ROUNDS - 1)




def kernel(**inputs):
    import numpy as _np
    import concourse.bacc as _bacc
    from concourse import mybir as _mybir
    from concourse.bass_utils import run_bass_kernel_spmd as _run

    x = {name: _np.asarray(a) for name, a in inputs.items()}
    w1 = x["W_top1"]
    given = {"dense": x["r_dense_features"], "ids": x["ids"]}
    given |= {f"table{f}": x[f"tbl_{f}"] for f in range(TABLES)}
    rounds = x["ids"].shape[0] // (2 * P)
    given["picked_ids"] = x["ids"][:, PICKED].reshape(P, rounds, 2, NP).transpose(3, 1, 2, 0).reshape(NP, rounds, 2 * P)
    given |= {"w1_pairs": w1[_np.array(pair_rows())],
              "w1_dense": _np.concatenate([w1[:P], w1[-P:]]),
              "b1": x["b_top1"], "w2": x["W_top2"], "b2": x["b_top2"], "w3": x["W_top3"],
              "eye": _np.eye(P, dtype=_np.float32),
              "row_of": _np.arange(ROWS, dtype=_np.float32).reshape(ROWS_PER_PART, PARTS)}
    nc = _bacc.Bacc("TRN2", target_bir_lowering=False, num_devices=1)
    aps, arrays = {}, {}
    for name, a in given.items():
        a = _np.ascontiguousarray(a)
        arrays[f"in_{name}"] = a
        aps[name] = nc.dram_tensor(f"in_{name}", a.shape, _mybir.dt.from_np(a.dtype), kind="ExternalInput").ap()
    out = nc.dram_tensor("out_y", (x["ids"].shape[0], 1), _mybir.dt.float32, kind="ExternalOutput").ap()
    dlrm_tower(nc, aps["dense"], aps["ids"], aps["picked_ids"], [aps[f"table{f}"] for f in range(TABLES)], aps["w1_pairs"],
               aps["w1_dense"], aps["b1"], aps["w2"], aps["b2"], aps["w3"], aps["eye"], aps["row_of"],
               out)
    r = _run(nc, [arrays], core_ids=[0])
    return r.results[0]["out_y"]
```
